# Optimizing a Trainium2 kernel written in Bass

```python
import numpy as np
import jax
import jax.numpy as jnp

def _softmax(x, axis=-1):
    return jax.nn.softmax(x, axis=axis)

def _gelu(x):
    return jax.nn.gelu(x, approximate=True)

def _silu(x):
    return jax.nn.silu(x)

def _sigmoid(x):
    return jax.nn.sigmoid(x)

def _layernorm(x, axis=-1, eps=1e-05):
    m = jnp.mean(x, axis=axis, keepdims=True)
    v = jnp.var(x, axis=axis, keepdims=True)
    return (x - m) / jnp.sqrt(v + eps)

def _scatter_add(tgt, idx, src, axis=0):
    return tgt.at[idx].add(src)

def _segment_sum(src, seg, n):
    return jax.ops.segment_sum(src, seg, n)
kernel_name = 'mk_flamingo_gated_d2_seqx_r8_1cfba3'

def setup_inputs(seed: int=0):
    np.random.seed(seed)
    _w = jnp.asarray

    def _rec_inputs():
        import jax
        import jax.numpy as jnp
        _rk = jax.random.key(seed)
        x = 0.0002417 + 0.9998 * jax.random.normal(jax.random.fold_in(_rk, 1), (8, 128, 128), jnp.float32)
        _lenS = 128 - jax.random.randint(jax.random.fold_in(_rk, 7), (8,), 0, max(1, 128 // 4) + 1, jnp.int32)
        _lenS2 = 77 - jax.random.randint(jax.random.fold_in(_rk, 8), (8,), 0, max(1, 77 // 4) + 1, jnp.int32)
        _ctx_1024P = jax.random.normal(jax.random.fold_in(_rk, 11), (8, 16, 128), jnp.float32)
        _ctx_1024c = jax.random.dirichlet(jax.random.fold_in(_rk, 511), 0.3 * jnp.ones((16,), jnp.float32), (8, 77))
        _ctx_1024t = jnp.einsum('bsk,bkd->bsd', _ctx_1024c, _ctx_1024P)
        _ctx_1024t = _ctx_1024t * jax.lax.rsqrt(jnp.mean(jnp.square(_ctx_1024t)) + 1e-12) * 0.953939
        ctx_1024 = -0.000125008 + 0.999885 * (_ctx_1024t + 0.3 * jax.random.normal(jax.random.fold_in(_rk, 611), (8, 77, 128), jnp.float32))
        _validS = jnp.arange(128)[None, :] < _lenS[:, None]
        _validS2 = jnp.arange(77)[None, :] < _lenS2[:, None]
        _causal = jnp.tril(jnp.ones((128, 128), dtype=bool))
        mask_BxSxS2_bk1 = jnp.broadcast_to(_validS2[:, None, :], (8, 128, 77))
        _g = jax.random.normal(jax.random.fold_in(_rk, 9001), (2, 2), jnp.float32)
        _g = jnp.sign(_g) * jnp.maximum(jnp.abs(_g), 1.0) + (_g == 0) * 1.0
        g_xattn = _g[0]
        g_ffn = _g[1]
        return (x, ctx_1024, mask_BxSxS2_bk1, g_xattn, g_ffn)
    x, ctx_1024, mask_BxSxS2_bk1, g_xattn, g_ffn = _rec_inputs()

    def _L0_xattn_setup():
        import jax, jax.numpy as jnp
        import numpy as np
        NEG_INF = -1000000000.0
        key = jax.random.key(seed)
        kv, kk, kq, km, kw, kb = jax.random.split(key, 6)
        B, Lq, Lk, D = (8, 128, 512, 128)
        v = jax.random.normal(kv, (B, Lk, D), dtype=jnp.float32)
        k = jax.random.normal(kk, (B, Lk, D), dtype=jnp.float32)
        q = jax.random.normal(kq, (B, Lq, D), dtype=jnp.float32)
        mask = jax.random.randint(km, (B, Lq, Lk), 0, 2) > 0
        W_merge = jax.random.normal(kw, (D, D), dtype=jnp.float32) / np.sqrt(D)
        b_merge = jax.random.normal(kb, (D,), dtype=jnp.float32) * 0.02
        return {'v': v, 'k': k, 'q': q, 'mask': mask, 'W_merge': W_merge, 'b_merge': b_merge}
    _L0_xattn_all = _L0_xattn_setup()
    _L0_xattn_in = {k: v for k, v in _L0_xattn_all.items() if k in ('W_merge', 'b_merge')}
    del _L0_xattn_all

    def _L0_ffn_setup():
        import jax, jax.numpy as jnp
        import numpy as np
        from jax import lax
        B, L, D = (4, 256, 128)
        E, TOPK = (8, 2)
        K, DIL = (3, 1)
        HID = D // 4
        EPS = 1e-06

        def _rmsnorm(h, w):
            rms = jnp.sqrt(jnp.mean(h * h, axis=-1, keepdims=True) + EPS)
            return w * (h / rms)

        def _forward(x, dw_kernel, dw_bias, pw_w, pw_b, router_w, router_b, expert_w, expert_b, out_w, out_b, norm_w, ff_down_w, ff_down_b, ff_up_w, ff_up_b):
            pad = (K - 1) * DIL
            xc = jnp.transpose(x, (0, 2, 1))
            xc = lax.conv_general_dilated(xc, dw_kernel, window_strides=(1,), padding=((pad, 0),), rhs_dilation=(DIL,), dimension_numbers=('NCH', 'OIH', 'NCH'), feature_group_count=D) + dw_bias[None, :, None]
            xc = jax.nn.silu(jnp.einsum('bdl,ed->bel', xc, pw_w) + pw_b[None, :, None])
            x1 = x + jnp.transpose(xc, (0, 2, 1))
            logits = jnp.einsum('bsd,ed->bse', x1, router_w) + router_b
            top_v, top_i = lax.top_k(logits, TOPK)
            top_w = jax.nn.softmax(top_v, axis=-1)
            rw = jnp.sum(jax.nn.one_hot(top_i, E, dtype=x1.dtype) * top_w[..., None], axis=-2)
            ye = jax.nn.silu(jnp.einsum('bsd,eod->bseo', x1, expert_w) + expert_b)
            combined = jnp.einsum('bse,bseo->bso', rw, ye)
            moe_out = jnp.einsum('bsd,od->bso', combined, out_w) + out_b
            h = _rmsnorm(x1 + moe_out, norm_w)
            ff = jax.nn.gelu(jnp.einsum('bsd,hd->bsh', h, ff_down_w) + ff_down_b, approximate=False)
            ff = jnp.einsum('bsh,dh->bsd', ff, ff_up_w) + ff_up_b
            return h + ff
        key = jax.random.key(seed)
        ks = jax.random.split(key, 16)
        s = 0.02
        return {'x': jax.random.normal(ks[0], (B, L, D), dtype=jnp.float32), 'dw_kernel': jax.random.normal(ks[1], (D, 1, K), dtype=jnp.float32) * s, 'dw_bias': jnp.zeros((D,), dtype=jnp.float32), 'pw_w': jax.random.normal(ks[2], (D, D), dtype=jnp.float32) * s, 'pw_b': jnp.zeros((D,), dtype=jnp.float32), 'router_w': jax.random.normal(ks[3], (E, D), dtype=jnp.float32) * s, 'router_b': jnp.zeros((E,), dtype=jnp.float32), 'expert_w': jax.random.normal(ks[4], (E, D, D), dtype=jnp.float32) * s, 'expert_b': jnp.zeros((E, D), dtype=jnp.float32), 'out_w': jax.random.normal(ks[5], (D, D), dtype=jnp.float32) * s, 'out_b': jnp.zeros((D,), dtype=jnp.float32), 'norm_w': jnp.ones((D,), dtype=jnp.float32), 'ff_down_w': jax.random.normal(ks[6], (HID, D), dtype=jnp.float32) * s, 'ff_down_b': jnp.zeros((HID,), dtype=jnp.float32), 'ff_up_w': jax.random.normal(ks[7], (D, HID), dtype=jnp.float32) * s, 'ff_up_b': jnp.zeros((D,), dtype=jnp.float32)}
    _L0_ffn_all = _L0_ffn_setup()
    _L0_ffn_in = {k: v for k, v in _L0_ffn_all.items() if k in ('dw_kernel', 'dw_bias', 'pw_w', 'pw_b', 'router_w', 'router_b', 'expert_w', 'expert_b', 'out_w', 'out_b', 'norm_w', 'ff_down_w', 'ff_down_b', 'ff_up_w', 'ff_up_b')}
    del _L0_ffn_all

    def _L1_xattn_setup():
        import jax, jax.numpy as jnp
        import numpy as np
        DIM_IN = 128
        DIM_QK = 128
        DIM_V = 128
        key = jax.random.key(seed)
        ks = jax.random.split(key, 8)
        s = DIM_IN ** (-0.5)
        return {'x': jax.random.normal(ks[0], (16, 256, DIM_IN), dtype=jnp.float32), 'encoder_output': jax.random.normal(ks[1], (16, 256, DIM_IN), dtype=jnp.float32), 'W_q': jax.random.normal(ks[2], (DIM_IN, DIM_QK), dtype=jnp.float32) * s, 'b_q': jnp.zeros((DIM_QK,), dtype=jnp.float32), 'W_k': jax.random.normal(ks[3], (DIM_IN, DIM_QK), dtype=jnp.float32) * s, 'b_k': jnp.zeros((DIM_QK,), dtype=jnp.float32), 'W_v': jax.random.normal(ks[4], (DIM_IN, DIM_V), dtype=jnp.float32) * s, 'b_v': jnp.zeros((DIM_V,), dtype=jnp.float32)}
    _L1_xattn_all = _L1_xattn_setup()
    _L1_xattn_in = {k: v for k, v in _L1_xattn_all.items() if k in ('W_q', 'b_q', 'W_k', 'b_k', 'W_v', 'b_v')}
    del _L1_xattn_all

    def _L1_ffn_setup():
        import jax, jax.numpy as jnp
        import numpy as np
        H = 128
        E = 64
        K = 8
        G = 8
        TOPK_GROUP = 4
        I_MOE = 64
        I_SHARED = 256
        SCALE = 2.5

        def relu2(x):
            return jnp.square(jax.nn.relu(x))

        def _route(xf, router_w, correction_bias):
            T = xf.shape[0]
            logits = xf @ router_w.T
            scores = jax.nn.sigmoid(logits)
            sfc = scores + correction_bias[None, :]
            grp = sfc.reshape(T, G, E // G)
            top2, _ = jax.lax.top_k(grp, 2)
            group_scores = top2.sum(-1)
            _, gidx = jax.lax.top_k(group_scores, TOPK_GROUP)
            gmask = jnp.zeros((T, G), sfc.dtype).at[jnp.arange(T)[:, None], gidx].set(1.0)
            emask = jnp.repeat(gmask, E // G, axis=1)
            masked = jnp.where(emask > 0, sfc, 0.0)
            _, tidx = jax.lax.top_k(masked, K)
            tw = jnp.take_along_axis(scores, tidx, axis=1)
            tw = tw / (tw.sum(-1, keepdims=True) + 1e-20)
            return (tidx, tw * SCALE)
        key = jax.random.key(seed)
        ks = jax.random.split(key, 7)
        x = jax.random.normal(ks[0], (2, 128, H), dtype=jnp.float32)
        router_w = jax.random.normal(ks[1], (E, H), dtype=jnp.float32) * 0.02
        correction_bias = jax.random.normal(ks[2], (E,), dtype=jnp.float32) * 0.01
        up_w = jax.random.normal(ks[3], (E, H, I_MOE), dtype=jnp.float32) * 0.02
        down_w = jax.random.normal(ks[4], (E, I_MOE, H), dtype=jnp.float32) * 0.02
        shared_up_w = jax.random.normal(ks[5], (H, I_SHARED), dtype=jnp.float32) * 0.02
        shared_down_w = jax.random.normal(ks[6], (I_SHARED, H), dtype=jnp.float32) * 0.02
        return {'x': x, 'router_w': router_w, 'correction_bias': correction_bias, 'up_w': up_w, 'down_w': down_w, 'shared_up_w': shared_up_w, 'shared_down_w': shared_down_w}
    _L1_ffn_all = _L1_ffn_setup()
    _L1_ffn_in = {k: v for k, v in _L1_ffn_all.items() if k in ('router_w', 'correction_bias', 'up_w', 'down_w', 'shared_up_w', 'shared_down_w')}
    del _L1_ffn_all
    return {'x': x, 'ctx_1024': ctx_1024, 'mask_BxSxS2_bk1': mask_BxSxS2_bk1, 'g_xattn': g_xattn, 'g_ffn': g_ffn, 'L0_xattn_W_merge': _L0_xattn_in['W_merge'], 'L0_xattn_b_merge': _L0_xattn_in['b_merge'], 'L0_ffn_dw_kernel': _L0_ffn_in['dw_kernel'], 'L0_ffn_dw_bias': _L0_ffn_in['dw_bias'], 'L0_ffn_pw_w': _L0_ffn_in['pw_w'], 'L0_ffn_pw_b': _L0_ffn_in['pw_b'], 'L0_ffn_router_w': _L0_ffn_in['router_w'], 'L0_ffn_router_b': _L0_ffn_in['router_b'], 'L0_ffn_expert_w': _L0_ffn_in['expert_w'], 'L0_ffn_expert_b': _L0_ffn_in['expert_b'], 'L0_ffn_out_w': _L0_ffn_in['out_w'], 'L0_ffn_out_b': _L0_ffn_in['out_b'], 'L0_ffn_norm_w': _L0_ffn_in['norm_w'], 'L0_ffn_ff_down_w': _L0_ffn_in['ff_down_w'], 'L0_ffn_ff_down_b': _L0_ffn_in['ff_down_b'], 'L0_ffn_ff_up_w': _L0_ffn_in['ff_up_w'], 'L0_ffn_ff_up_b': _L0_ffn_in['ff_up_b'], 'L1_xattn_W_q': _L1_xattn_in['W_q'], 'L1_xattn_b_q': _L1_xattn_in['b_q'], 'L1_xattn_W_k': _L1_xattn_in['W_k'], 'L1_xattn_b_k': _L1_xattn_in['b_k'], 'L1_xattn_W_v': _L1_xattn_in['W_v'], 'L1_xattn_b_v': _L1_xattn_in['b_v'], 'L1_ffn_router_w': _L1_ffn_in['router_w'], 'L1_ffn_correction_bias': _L1_ffn_in['correction_bias'], 'L1_ffn_up_w': _L1_ffn_in['up_w'], 'L1_ffn_down_w': _L1_ffn_in['down_w'], 'L1_ffn_shared_up_w': _L1_ffn_in['shared_up_w'], 'L1_ffn_shared_down_w': _L1_ffn_in['shared_down_w']}

def reference(x, ctx_1024, mask_BxSxS2_bk1, g_xattn, g_ffn, L0_xattn_W_merge, L0_xattn_b_merge, L0_ffn_dw_kernel, L0_ffn_dw_bias, L0_ffn_pw_w, L0_ffn_pw_b, L0_ffn_router_w, L0_ffn_router_b, L0_ffn_expert_w, L0_ffn_expert_b, L0_ffn_out_w, L0_ffn_out_b, L0_ffn_norm_w, L0_ffn_ff_down_w, L0_ffn_ff_down_b, L0_ffn_ff_up_w, L0_ffn_ff_up_b, L1_xattn_W_q, L1_xattn_b_q, L1_xattn_W_k, L1_xattn_b_k, L1_xattn_W_v, L1_xattn_b_v, L1_ffn_router_w, L1_ffn_correction_bias, L1_ffn_up_w, L1_ffn_down_w, L1_ffn_shared_up_w, L1_ffn_shared_down_w):
    import jax
    import jax.numpy as jnp

    def _L0_xattn_ref(v, k, q, mask, W_merge, b_merge):
        import jax, jax.numpy as jnp
        import numpy as np
        NEG_INF = -1000000000.0
        d_k = q.shape[-1]
        scale = 1.0 / jnp.sqrt(jnp.asarray(d_k, dtype=q.dtype))
        scores = jnp.einsum('bqd,bkd->bqk', q, k) * scale
        scores = jnp.where(mask, jnp.asarray(NEG_INF, dtype=scores.dtype), scores)
        att_map = jax.nn.softmax(scores, axis=-1)
        atted = jnp.einsum('bqk,bkd->bqd', att_map, v)
        atted = jnp.swapaxes(atted, -1, -2)
        return jnp.einsum('bdl,ol->bdo', atted, W_merge) + b_merge

    def _L0_ffn_ref(x, dw_kernel, dw_bias, pw_w, pw_b, router_w, router_b, expert_w, expert_b, out_w, out_b, norm_w, ff_down_w, ff_down_b, ff_up_w, ff_up_b):
        import jax, jax.numpy as jnp
        import numpy as np
        from jax import lax
        B, L, D = (4, 256, 128)
        E, TOPK = (8, 2)
        K, DIL = (3, 1)
        HID = D // 4
        EPS = 1e-06

        def _rmsnorm(h, w):
            rms = jnp.sqrt(jnp.mean(h * h, axis=-1, keepdims=True) + EPS)
            return w * (h / rms)

        def _forward(x, dw_kernel, dw_bias, pw_w, pw_b, router_w, router_b, expert_w, expert_b, out_w, out_b, norm_w, ff_down_w, ff_down_b, ff_up_w, ff_up_b):
            pad = (K - 1) * DIL
            xc = jnp.transpose(x, (0, 2, 1))
            xc = lax.conv_general_dilated(xc, dw_kernel, window_strides=(1,), padding=((pad, 0),), rhs_dilation=(DIL,), dimension_numbers=('NCH', 'OIH', 'NCH'), feature_group_count=D) + dw_bias[None, :, None]
            xc = jax.nn.silu(jnp.einsum('bdl,ed->bel', xc, pw_w) + pw_b[None, :, None])
            x1 = x + jnp.transpose(xc, (0, 2, 1))
            logits = jnp.einsum('bsd,ed->bse', x1, router_w) + router_b
            top_v, top_i = lax.top_k(logits, TOPK)
            top_w = jax.nn.softmax(top_v, axis=-1)
            rw = jnp.sum(jax.nn.one_hot(top_i, E, dtype=x1.dtype) * top_w[..., None], axis=-2)
            ye = jax.nn.silu(jnp.einsum('bsd,eod->bseo', x1, expert_w) + expert_b)
            combined = jnp.einsum('bse,bseo->bso', rw, ye)
            moe_out = jnp.einsum('bsd,od->bso', combined, out_w) + out_b
            h = _rmsnorm(x1 + moe_out, norm_w)
            ff = jax.nn.gelu(jnp.einsum('bsd,hd->bsh', h, ff_down_w) + ff_down_b, approximate=False)
            ff = jnp.einsum('bsh,dh->bsd', ff, ff_up_w) + ff_up_b
            return h + ff
        return _forward(x, dw_kernel, dw_bias, pw_w, pw_b, router_w, router_b, expert_w, expert_b, out_w, out_b, norm_w, ff_down_w, ff_down_b, ff_up_w, ff_up_b)

    def _L1_xattn_ref(x, encoder_output, W_q, b_q, W_k, b_k, W_v, b_v):
        import jax, jax.numpy as jnp
        import numpy as np
        DIM_IN = 128
        DIM_QK = 128
        DIM_V = 128
        Q = x @ W_q + b_q
        K = encoder_output @ W_k + b_k
        V = encoder_output @ W_v + b_v
        scores = jnp.einsum('bqd,bkd->bqk', Q, K) * K.shape[-1] ** (-0.5)
        weights = jax.nn.softmax(scores, axis=-1)
        H = jnp.einsum('bqk,bkv->bqv', weights, V)
        return H

    def _L1_ffn_ref(x, router_w, correction_bias, up_w, down_w, shared_up_w, shared_down_w):
        import jax, jax.numpy as jnp
        import numpy as np
        H = 128
        E = 64
        K = 8
        G = 8
        TOPK_GROUP = 4
        I_MOE = 64
        I_SHARED = 256
        SCALE = 2.5

        def relu2(x):
            return jnp.square(jax.nn.relu(x))

        def _route(xf, router_w, correction_bias):
            T = xf.shape[0]
            logits = xf @ router_w.T
            scores = jax.nn.sigmoid(logits)
            sfc = scores + correction_bias[None, :]
            grp = sfc.reshape(T, G, E // G)
            top2, _ = jax.lax.top_k(grp, 2)
            group_scores = top2.sum(-1)
            _, gidx = jax.lax.top_k(group_scores, TOPK_GROUP)
            gmask = jnp.zeros((T, G), sfc.dtype).at[jnp.arange(T)[:, None], gidx].set(1.0)
            emask = jnp.repeat(gmask, E // G, axis=1)
            masked = jnp.where(emask > 0, sfc, 0.0)
            _, tidx = jax.lax.top_k(masked, K)
            tw = jnp.take_along_axis(scores, tidx, axis=1)
            tw = tw / (tw.sum(-1, keepdims=True) + 1e-20)
            return (tidx, tw * SCALE)
        B, S, Hd = x.shape
        xf = x.reshape(-1, Hd)
        T = xf.shape[0]
        tidx, tw = _route(xf.astype(jnp.float32), router_w, correction_bias)
        combine = jnp.zeros((T, E), xf.dtype).at[jnp.arange(T)[:, None], tidx].add(tw.astype(xf.dtype))

        def body(acc, ew):
            wu, wd, c = ew
            return (acc + c[:, None] * (relu2(xf @ wu) @ wd), None)
        routed, _ = jax.lax.scan(body, jnp.zeros_like(xf), (up_w, down_w, combine.T))
        shared = relu2(xf @ shared_up_w) @ shared_down_w
        return (routed + shared).reshape(B, S, Hd)
    x = x + jnp.tanh(g_xattn[0]) * _L0_xattn_ref(ctx_1024, ctx_1024, _layernorm(x, axis=-1), mask_BxSxS2_bk1, L0_xattn_W_merge, L0_xattn_b_merge)
    x = x + jnp.tanh(g_ffn[0]) * _L0_ffn_ref(_layernorm(x, axis=-1), L0_ffn_dw_kernel, L0_ffn_dw_bias, L0_ffn_pw_w, L0_ffn_pw_b, L0_ffn_router_w, L0_ffn_router_b, L0_ffn_expert_w, L0_ffn_expert_b, L0_ffn_out_w, L0_ffn_out_b, L0_ffn_norm_w, L0_ffn_ff_down_w, L0_ffn_ff_down_b, L0_ffn_ff_up_w, L0_ffn_ff_up_b)
    x = x + jnp.tanh(g_xattn[1]) * _L1_xattn_ref(_layernorm(x, axis=-1), ctx_1024, L1_xattn_W_q, L1_xattn_b_q, L1_xattn_W_k, L1_xattn_b_k, L1_xattn_W_v, L1_xattn_b_v)
    x = x + jnp.tanh(g_ffn[1]) * _L1_ffn_ref(_layernorm(x, axis=-1), L1_ffn_router_w, L1_ffn_correction_bias, L1_ffn_up_w, L1_ffn_down_w, L1_ffn_shared_up_w, L1_ffn_shared_down_w)
    return x

_drawn_inputs = setup_inputs


def setup_inputs(seed=0):
    import zlib

    import numpy as np

    out = dict(_drawn_inputs(seed))
    spreads = {'g_ffn': (-1.0, 0.6),
     'L0_ffn_dw_bias': (0.0, 0.51),
     'L0_ffn_pw_b': (0.0, 0.1),
     'L0_ffn_router_b': (0.0, 0.492),
     'L0_ffn_expert_b': (0.0, 0.685),
     'L0_ffn_out_b': (0.0, 0.1),
     'L0_ffn_norm_w': (1.0, 0.2),
     'L0_ffn_ff_down_b': (0.0, 0.768),
     'L0_ffn_ff_up_b': (0.0, 0.1),
     'L1_xattn_b_q': (0.0, 0.328),
     'L1_xattn_b_k': (0.0, 2.0),
     'L1_xattn_b_v': (0.0, 0.1)}
    factors = {'L0_xattn_b_merge': 5.168,
     'L0_ffn_dw_kernel': 8.0,
     'L0_ffn_pw_w': 3.709,
     'L0_ffn_ff_down_w': 2.877,
     'L1_ffn_router_w': 5.797,
     'L1_ffn_correction_bias': 8.0,
     'L1_ffn_up_w': 5.737,
     'L1_ffn_down_w': 5.343,
     'L1_ffn_shared_up_w': 5.715,
     'L1_ffn_shared_down_w': 5.371}
    for name, (base, spread) in spreads.items():
        noise = np.random.default_rng([zlib.crc32(name.encode()), seed]).standard_normal(out[name].shape)
        drawn = base * np.exp(spread * noise) if base else spread * noise
        out[name] = jnp.asarray(drawn.astype(out[name].dtype))
    for name, factor in factors.items():
        out[name] = (out[name] * factor).astype(out[name].dtype)
    return out
```

```python
from contextlib import ExitStack

import concourse.bass as bass
from concourse import mybir

F32 = mybir.dt.float32
F32R = mybir.dt.float32r
I32 = mybir.dt.int32
U8 = mybir.dt.uint8
ALU = mybir.AluOpType
ACT = mybir.ActivationFunctionType
AX_X = mybir.AxisListType.X

P = 128
NEG_INF = -1e9
PAD = -3.0e38
PICKED = 3.0e38
IS_PICKED = 1.0e38
RSQRT_MAGIC = float(0x5F3759DF)

FRONT = 22


def expert_items(groups):
    items = []
    for g in range(groups + 2):
        step = []
        if g < groups:
            step.append(("up", g))
        if 1 <= g <= groups:
            step.append(("tr", g - 1))
        if g >= 2:
            step.append(("down", g - 2))
        items.append(step)
    return items


def merged_items(groups):
    steps = [item for step in expert_items(groups) for item in step]
    out, placed = [], 0
    for n, item in enumerate(steps):
        out.append(item)
        while placed < FRONT - 1 and placed * len(steps) < (n + 1) * (FRONT - 1):
            out.append(("f", placed))
            placed += 1
    return out + [("f", FRONT - 1)]


def flamingo_kernel(
    nc, x, ctx_1024, mask, g_xattn, g_ffn, W_merge, b_merge, dw_kernel, dw_bias, pw_w, pw_b,
    router0_w, router0_b, expert_w, expert_b, out_w, out_b, norm_w, ff_down_w, ff_down_b, ff_up_w,
    ff_up_b, W_q, b_q, W_k, b_k, W_v, b_v, router1_w, correction_bias, up_w, down_w, shared_up_w,
    shared_down_w, out,
):
    B, L, D = x.shape
    LK = ctx_1024.shape[1]
    E0 = expert_w.shape[0]
    E1, _, HI = up_w.shape
    SH = shared_up_w.shape[1]
    KD = dw_kernel.shape[2]
    HID = ff_down_w.shape[0]
    T = 2
    STEPS = B // T
    N = T * P
    G8 = 8
    EG = E1 // G8
    TOPG = 4
    GW = 512
    EPG = GW // HI
    GROUPS = (E1 * HI + SH + GW - 1) // GW
    ROUTED = E1 * HI // GW
    NBLK = (E1 * HI + SH) // P
    HW = E1 * HI + SH
    SCALE = float(D) ** -0.5
    assert L == P and D == P and LK <= P and T * GW // 4 <= 512 and KD == 3

    def blocks_of(g):
        return range(g * (GW // P), min((g + 1) * (GW // P), NBLK))

    with ExitStack() as ctx:
        def sb(name, shape, dt=F32):
            return ctx.enter_context(nc.sbuf_tensor(name, shape, dt))

        def bank(name):
            return ctx.enter_context(nc.psum_tensor(name, [P, 512], F32))

        ident = sb("ident", [P, P])
        ident_r = sb("ident_r", [P, P], F32R)
        stage_w = sb("stage_w", [P, 8, P])
        stage_e = sb("stage_e", [P, E0, P])
        merge_T = sb("merge_T", [P, P])
        pw_T = sb("pw_T", [P, P])
        outw_T = sb("outw_T", [P, P])
        ffd_T = sb("ffd_T", [P, HID])
        ffu_T = sb("ffu_T", [HID, P])
        r0_hi = sb("r0_hi", [P, E0], F32R)
        r0_lo = sb("r0_lo", [P, E0], F32R)
        r1_hi = sb("r1_hi", [P, E1], F32R)
        r1_lo = sb("r1_lo", [P, E1], F32R)
        exp_hi = sb("exp_hi", [P, E0 * P], F32R)
        exp_lo = sb("exp_lo", [P, E0 * P], F32R)
        wq = sb("wq", [P, P])
        wk = sb("wk", [P, P])
        wv = sb("wv", [P, P])
        up_sb = sb("up_sb", [P, HW])
        up_hi = sb("up_hi", [P, HW], F32R)
        up_lo = sb("up_lo", [P, HW], F32R)
        down_sb = sb("down_sb", [P, NBLK, P])
        gates = sb("gates", [P, 4])
        tg = sb("tg", [P, 4])
        rows = sb("rows", [P, 5, P])
        grows = sb("grows", [P, 3, P])
        r0b = sb("r0b", [P, E0])
        r1b = sb("r1b", [P, E1])
        dwk = sb("dwk", [P, KD])
        dwb = sb("dwb", [P, 1])
        pwb = sb("pwb", [P, 2])
        fdb = sb("fdb", [HID, 1])
        bq = sb("bq", [P, 1])
        bk = sb("bk", [P, 1])
        eb = sb("eb", [2, E0 * P])
        eb_hi = sb("eb_hi", [2, E0 * P], F32R)
        eb2 = sb("eb2", [2, E0 * P], F32R)
        neg_row1 = sb("neg_row1", [2, 1])
        ones2f = sb("ones2f", [2, P])
        ones2 = sb("ones2", [2, P], F32R)
        neg_inf = sb("neg_inf", [P, T, LK])
        neg_half = sb("neg_half", [P, T])

        x_in = sb("x_in", [P, T, P])
        ctx_in = sb("ctx_in", [LK, T, P])
        mask_in = sb("mask_in", [P, T, LK], U8)
        bn = sb("bn", [P, T, 6])
        mv = sb("mv", [P, T, 2])
        veps = sb("veps", [P, T])
        rstd = sb("rstd", [P, T])
        q_tok = sb("q_tok", [P, T, P])
        qT = sb("qT", [P, N])
        ctxT = sb("ctxT", [P, T * LK])
        KT = sb("KT", [P, T * LK])
        V = sb("V", [LK, T, P])
        att = sb("att", [P, T, LK])
        mx = sb("mx", [P, T])
        nmx = sb("nmx", [P, T])
        psum_t = sb("psum_t", [P, T])
        rs = sb("rs", [P, T])
        G = sb("G", [LK, T, P])
        xb = sb("xb", [P, T, P])
        x1 = sb("x1", [P, T, P])
        x1b = sb("x1b", [P, T, P])
        ucv = sb("ucv", [P, T, P + KD - 1])
        cv = sb("cv", [P, T, P])
        th = sb("th", [P, N])
        zh = sb("zh", [P, N])
        yT = sb("yT", [P, N])
        y_hi = sb("y_hi", [P, N], F32R)
        y_lo = sb("y_lo", [P, N], F32R)
        lv = sb("lv", [P, T, 16])
        top = sb("top", [P, T, 32])
        mr = sb("mr", [P, T, 16])
        rw = sb("rw", [P, T, E0])
        eth = sb("eth", [P, 2, 512])
        eg = sb("eg", [P, 2, 512])
        ew = sb("ew", [P, T, E0 * P])
        acc0 = sb("acc0", [P, T, P])
        combT = sb("combT", [P, N])
        hp = sb("hp", [P, T, P])
        sq = sb("sq", [P, T, P])
        ssq = sb("ssq", [P, T])
        h = sb("h", [P, T, P])
        hT = sb("hT", [P, N])
        gl = sb("gl", [HID, N])
        x2 = sb("x2", [P, T, P])
        x2b = sb("x2b", [P, T, P])
        QT = sb("QT", [P, N])
        PT = sb("PT", [LK, T, P])
        x3 = sb("x3", [P, T, P])
        xf = sb("xf", [P, T, P])
        sg = sb("sg", [P, T, E1])
        sfc = sb("sfc", [P, T, E1])
        g8 = sb("g8", [P, T, G8, 8])
        gv = sb("gv", [P, T, 16])
        gtop = sb("gtop", [P, T, 16])
        gmr = sb("gmr", [P, T, 16])
        masked = sb("masked", [P, T, E1])
        etop = sb("etop", [P, T, 8])
        emr = sb("emr", [P, T, E1])
        cw = sb("cw", [P, T, E1])
        cs = sb("cs", [P, T])
        ry = sb("ry", [P, T, E1])
        ra = sb("ra", [P, T, E1])
        rb = sb("rb", [P, T, E1])

        x_hi = sb("x_hi", [P, N], F32R)
        x_lo = sb("x_lo", [P, N], F32R)
        x3m = sb("x3m", [P, T, P])
        sc = sb("sc", [P, T, E1])

        u = sb("u", [P, 2, T, GW])
        hid = sb("hid", [P, 2, GW // P, N])
        accs = sb("accs", [P, N])
        y_out = sb("y_out", [P, T, P])

        acc_bank = bank("acc_bank")
        z_bank = [bank(f"z_bank{t}") for t in range(2)]
        uT_bank = [bank(f"uT_bank{j}") for j in range(2)]
        F = [bank(f"front{j}") for j in range(3)]

        per = {
            "in_loaded": 48, "ln_var": 5, "ln_rstd": 5,
            "q_ready": 1, "q_T": 1, "ctx_T": 1, "qT_copied": 1, "ctxT_copied": 1, "kv_done": 1, "kv_copied": 2,
            "scores": 1, "scores_masked": 1, "att_exp": 1, "att_ready": 1, "G_done": 1, "G_copied": 1,
            "Y_done": 1, "xb_ready": 1, "x1_ready": 1, "u_ready": 1, "u_T": 1, "conv_ready": 1, "pw_done": 1,
            "pw_tanh": 2, "y_ready": 1, "logits0": 1, "lmax_ready": 1, "lexp": 1,
            "ez_done": 4, "ez_tanh": 4, "eg_ready": 4, "ew_ready": 4, "rw_ready": 1, "comb_ready": 1,
            "comb_T": 1, "comb_copied": 1, "hp_done": 1, "hp_ready": 1, "ssq_ready": 1, "h_ready": 1,
            "h_T": 1, "hT_copied": 1, "ffd_done": 1, "gelu_ready": 1, "ffu_done": 1, "x1b_ready": 1,
            "x2_ready": 1, "x2b_ready": 1, "q2_ready": 1, "q2_T": 1, "q2T_copied": 1, "QT_done": 1,
            "QT_copied": 1, "scores2": 1, "max2_ready": 1, "exp2": 1, "P_T": 1, "PT_copied": 1,
            "H_done": 1, "x3_ready": 1, "xf_ready": 1, "xf_T": 1, "x_split": 1, "logits1": 1, "nexp": 1,
            "sc_ready": 1, "x3m_ready": 1,
            "z_done": GROUPS * T, "u_done": GROUPS * T, "uT_done": 2 * (GROUPS - 1) + 1,
            "hid_done": 2 * (GROUPS - 1) + 1, "down_done": GROUPS, "acc_copied": 1, "acc_T": 1, "out_ready": 1,
            "stored": 16,
        }
        sems = {name: ctx.enter_context(nc.semaphore(name)) for name in per}
        one = {}
        for name in ("w_loaded", "c_loaded", "e_loaded", "u_loaded", "d_loaded", "ident_ready", "consts", "w_T", "w_copied", "e_T", "e_hi", "e_lo",
                     "up_h", "up_l", "eb_split", "identr_ready", "gate_ready", "rows_ready", "dve_chain", "pool_setup"):
            one[name] = ctx.enter_context(nc.semaphore(name))

        def wait(eng, name, p, k=None):
            value = p * per[name] + (per[name] if k is None else k)
            if not isinstance(value, int) or value > 0:
                eng.wait_ge(sems[name], value)

        def signal(instruction, name):
            instruction.then_inc(sems[name], 16 if name in ("in_loaded", "stored") else 1)

        def run(eng, front, expert):
            for k in range(FRONT):
                front(k, 0)
            with eng.Fori(0, STEPS - 1) as i:
                for what, n in merged_items(GROUPS):
                    if what == "f":
                        front(n, i + 1)
                    else:
                        expert(what, n, i)
            for step in expert_items(GROUPS):
                for what, n in step:
                    expert(what, n, STEPS - 1)

        W_MERGE, W_PW, W_OUT, W_FFD, W_FFU, W_R0, W_R1 = range(7)
        small_T = [(W_MERGE, P, P), (W_PW, P, P), (W_OUT, P, P), (W_FFD, HID, P), (W_FFU, P, HID),
                   (W_R0, E0, P), (W_R1, E1, P)]

        UP_SPLIT_AT = [4, 8, 12, 16]

        def up_part(n):
            w = HW // len(UP_SPLIT_AT)
            return slice(n * w, (n + 1) * w)

        block = ctx.enter_context(nc.Block())

        @block.sync
        def _(sp):
            def load_pair(p):
                wait(sp, "x1_ready", p - 1)
                for dst, src in ((x_in, x), (ctx_in, ctx_1024), (mask_in, mask)):
                    signal(sp.dma_start(dst[:], src[bass.ds(p * T, T)].rearrange("t s c -> s t c")), "in_loaded")

            def load(dst, src, name):
                sp.dma_start(dst, src).then_inc(one[name], 16)

            load_pair(0)
            load(stage_w[:, W_MERGE, :], W_merge, "w_loaded")
            load(stage_w[:, W_PW, :], pw_w, "w_loaded")
            load(stage_w[:, W_OUT, :], out_w, "w_loaded")
            load(stage_w[0:HID, W_FFD, :], ff_down_w, "w_loaded")
            load(stage_w[:, W_FFU, 0:HID], ff_up_w, "w_loaded")
            load(stage_w[0:E0, W_R0, :], router0_w, "w_loaded")
            load(stage_w[0:E1, W_R1, :], router1_w, "w_loaded")
            load(stage_e[:], expert_w.rearrange("e o d -> o e d"), "e_loaded")
            load(up_sb[:, 0:E1 * HI].rearrange("d (e i) -> d e i", e=E1), up_w.rearrange("e d i -> d e i"), "u_loaded")
            load(up_sb[:, E1 * HI:HW], shared_up_w, "u_loaded")
            per_blk = P // HI
            for e in range(per_blk):
                load(down_sb[e * HI:(e + 1) * HI, 0:E1 // per_blk, :],
                     down_w.rearrange("(b e) i d -> e i b d", e=per_blk)[e], "d_loaded")
            load(down_sb[:, E1 // per_blk:NBLK, :], shared_down_w.rearrange("(b i) d -> i b d", i=P), "d_loaded")
            with sp.Fori(1, STEPS) as p:
                load_pair(p)

        @block.gpsimd
        def _(pool):
            nc.gpsimd.memset(ident[:], 0.0).then_inc(one["pool_setup"], 1)
            nc.gpsimd.memset(neg_row1[:], 0.0).then_inc(one["pool_setup"], 1)
            nc.gpsimd.memset(neg_half[:], -0.5).then_inc(one["pool_setup"], 1)
            pool.wait_ge(one["pool_setup"], 3)
            nc.gpsimd.affine_select(out=ident[:], in_=ident[:], compare_op=ALU.not_equal, fill=1.0, base=0,
                                    pattern=[[-1, P]], channel_multiplier=1).then_inc(one["ident_ready"], 1)
            nc.gpsimd.affine_select(out=neg_row1[:], in_=neg_row1[:], compare_op=ALU.not_equal, fill=-1.0, base=-1,
                                    pattern=[[0, 1]], channel_multiplier=1).then_inc(one["ident_ready"], 1)
            nc.gpsimd.memset(ones2f[:], 1.0).then_inc(one["consts"], 1)
            nc.gpsimd.memset(neg_inf[:], NEG_INF).then_inc(one["consts"], 1)
            nc.gpsimd.memset(ucv[:], 0.0).then_inc(one["consts"], 1)
            nc.gpsimd.memset(lv[:], PAD).then_inc(one["consts"], 1)
            nc.gpsimd.memset(top[:], PAD).then_inc(one["consts"], 1)
            nc.gpsimd.memset(gv[:], PAD).then_inc(one["consts"], 1)
            nc.gpsimd.memset(gtop[:], PAD).then_inc(one["consts"], 1)
            pool.wait_ge(one["gate_ready"], 1)
            pool.wait_ge(one["rows_ready"], 1)

            def power(n, p, half):
                wait(pool, "ln_var", p, n + 1)
                signal(nc.gpsimd.tensor_tensor(rstd[:], veps[:], half[:], ALU.pow), "ln_rstd")

            def front(k, p):
                if isinstance(p, int) and k in UP_SPLIT_AT:
                    n = UP_SPLIT_AT.index(k)
                    pool.wait_ge(one["up_h"], n + 1)
                    nc.gpsimd.tensor_tensor(up_lo[:, up_part(n)], up_sb[:, up_part(n)],
                                            up_hi[:, up_part(n)].bitcast(F32), ALU.subtract).then_inc(one["up_l"], 1)
                if k == 0:
                    power(0, p, neg_half)
                elif k == 3:
                    wait(pool, "in_loaded", p)
                    signal(nc.gpsimd.tensor_tensor(xb[:], x_in[:], grows[:, 0:1, :].broadcast_to([P, T, P]), ALU.add), "xb_ready")
                elif k == 5:
                    power(1, p, neg_half)
                    wait(pool, "x1_ready", p)
                    signal(nc.gpsimd.tensor_tensor(x1b[:], x1[:], grows[:, 1:2, :].broadcast_to([P, T, P]), ALU.add), "x1b_ready")
                elif k == 9:
                    wait(pool, "rw_ready", p)
                    for c in range(2 * T):
                        t, half = divmod(c, 2)
                        wait(pool, "eg_ready", p, c + 1)
                        signal(nc.gpsimd.tensor_tensor(
                            ew[:, t, half * 512:(half + 1) * 512].rearrange("p (e o) -> p e o", o=P),
                            eg[:, c % 2, :].rearrange("p (e o) -> p e o", o=P),
                            rw[:, t, half * 4:half * 4 + 4].unsqueeze(2).broadcast_to([P, 4, P]), ALU.mult), "ew_ready")
                elif k == 11:
                    power(2, p, neg_half)
                elif k == 14:
                    power(3, p, neg_half)
                    wait(pool, "x2_ready", p)
                    signal(nc.gpsimd.tensor_tensor(x2b[:], x2[:], grows[:, 2:3, :].broadcast_to([P, T, P]), ALU.add), "x2b_ready")
                elif k == 18:
                    power(4, p, neg_half)

            def expert(what, g, p):
                pass

            run(pool, front, expert)

        @block.scalar
        def _(act):
            def load(dst, src):
                act.dma_start(dst, src).then_inc(one["c_loaded"], 16)

            def row(src):
                return src.rearrange("(a n) -> a n", a=1)

            loads = [
                (gates[:, 0:2], row(g_xattn).broadcast_to([P, 2])), (gates[:, 2:4], row(g_ffn).broadcast_to([P, 2])),
                (rows[:, 0, :], row(b_merge).broadcast_to([P, P])), (rows[:, 1, :], row(out_b).broadcast_to([P, P])),
                (rows[:, 2, :], row(norm_w).broadcast_to([P, P])), (rows[:, 3, :], row(ff_up_b).broadcast_to([P, P])),
                (rows[:, 4, :], row(b_v).broadcast_to([P, P])), (r0b[:], row(router0_b).broadcast_to([P, E0])),
                (r1b[:], row(correction_bias).broadcast_to([P, E1])),
                (eb[:], expert_b.rearrange("(a e) o -> a (e o)", a=1).broadcast_to([2, E0 * P])),
                (dwk[:], dw_kernel.rearrange("d a k -> d (a k)")),
                (dwb[:], dw_bias.rearrange("(n a) -> n a", a=1)), (pwb[:, 0:1], pw_b.rearrange("(n a) -> n a", a=1)),
                (fdb[:], ff_down_b.rearrange("(n a) -> n a", a=1)), (bq[:], b_q.rearrange("(n a) -> n a", a=1)),
                (bk[:], b_k.rearrange("(n a) -> n a", a=1)), (wq[:], W_q), (wk[:], W_k), (wv[:], W_v),
            ]
            for dst, src in loads:
                load(dst, src)
            act.wait_ge(one["c_loaded"], 16 * len(loads))
            nc.scalar.activation(tg[:], gates[:], ACT.Tanh).then_inc(one["gate_ready"], 1)
            for c in range(2):
                act.wait_ge(one["e_T"], c + 1)
                nc.scalar.copy(exp_hi[:, c * 512:(c + 1) * 512], z_bank[c][:]).then_inc(one["e_hi"], 1)
            act.sem_inc(sems["stored"], 16)

            def front(k, p):
                if isinstance(p, int) and k in UP_SPLIT_AT:
                    n = UP_SPLIT_AT.index(k)
                    act.wait_ge(one["u_loaded"], 32)
                    nc.scalar.copy(up_hi[:, up_part(n)], up_sb[:, up_part(n)]).then_inc(one["up_h"], 1)
                if k == 1:
                    wait(act, "ctx_T", p)
                    signal(nc.scalar.copy(ctxT[:], F[1][:, 0:T * LK]), "ctxT_copied")
                elif k == 2:
                    wait(act, "scores_masked", p)
                    for t in range(T):
                        last = nc.scalar.activation(att[:, t, :], att[:, t, :], ACT.Exp, bias=nmx[:, t:t + 1],
                                                    accum_out=psum_t[:, t:t + 1])
                    signal(last, "att_exp")
                    wait(act, "kv_done", p)
                    signal(nc.scalar.activation(KT[:], F[0][:, 0:T * LK], ACT.Identity, bias=bk[:]), "kv_copied")
                    signal(nc.scalar.copy(V[:], F[1][0:LK, 0:N].rearrange("k (t d) -> k t d", t=T)), "kv_copied")
                elif k == 3:
                    wait(act, "G_done", p)
                    signal(nc.scalar.copy(G[:], F[2][0:LK, 0:N].rearrange("k (t d) -> k t d", t=T)), "G_copied")
                elif k == 7:
                    wait(act, "pw_done", p)
                    signal(nc.scalar.activation(th[:], F[1][:, 0:N], ACT.Tanh, bias=pwb[:, 1:2], scale=0.5), "pw_tanh")
                    signal(nc.scalar.activation(zh[:], F[1][:, 0:N], ACT.Identity, bias=pwb[:, 1:2], scale=0.5), "pw_tanh")
                elif k == 8:
                    wait(act, "lmax_ready", p)
                    signal(nc.scalar.activation(rw[:], rw[:], ACT.Exp), "lexp")
                elif k == 9:
                    for c in range(2 * T):
                        wait(act, "ez_done", p, c + 1)
                        if c >= 2:
                            wait(act, "eg_ready", p, c - 1)
                        signal(nc.scalar.activation(eth[:, c % 2, :], F[c % 2][:], ACT.Tanh, scale=0.5), "ez_tanh")
                elif k == 10:
                    wait(act, "comb_T", p)
                    signal(nc.scalar.copy(combT[:], F[2][:, 0:N]), "comb_copied")
                elif k == 11:
                    wait(act, "hp_ready", p)
                    for t in range(T):
                        last = nc.scalar.activation(sq[:, t, :], hp[:, t, :], ACT.Square, accum_out=ssq[:, t:t + 1])
                    signal(last, "ssq_ready")
                elif k == 12:
                    wait(act, "h_T", p)
                    signal(nc.scalar.copy(hT[:], F[1][:, 0:N]), "hT_copied")
                elif k == 13:
                    wait(act, "ffd_done", p)
                    signal(nc.scalar.activation(gl[:], F[2][0:HID, 0:N], ACT.Gelu, bias=fdb[:]), "gelu_ready")
                elif k == 15:
                    wait(act, "q2_T", p)
                    signal(nc.scalar.copy(qT[:], F[1][:, 0:N]), "q2T_copied")
                    wait(act, "QT_done", p)
                    signal(nc.scalar.activation(QT[:], F[2][:, 0:N], ACT.Identity, bias=bq[:]), "QT_copied")
                elif k == 16:
                    wait(act, "max2_ready", p)
                    for t in range(T):
                        last = nc.scalar.activation(att[:, t, :], F[0][:, t * LK:(t + 1) * LK], ACT.Exp, bias=nmx[:, t:t + 1],
                                                    scale=SCALE, accum_out=psum_t[:, t:t + 1])
                    signal(last, "exp2")
                elif k == 17:
                    wait(act, "P_T", p)
                    signal(nc.scalar.copy(PT[:], F[1][0:LK, 0:N].rearrange("k (t q) -> k t q", t=T)), "PT_copied")
                elif k == 19:
                    wait(act, "logits1", p)
                    signal(nc.scalar.activation(sg[:], F[0][:, 0:T * E1].rearrange("p (t e) -> p t e", t=T), ACT.Exp, scale=-1.0), "nexp")

            def expert(what, g, p):
                if what == "tr":
                    nb = len(blocks_of(g))
                    for a in range((nb + 1) // 2):
                        wait(act, "uT_done", p, 2 * g + a + 1)
                        if g >= 2:
                            wait(act, "down_done", p, g - 1)
                        signal(nc.scalar.activation(hid[:, g % 2, 2 * a:2 * a + 2, :],
                                                    uT_bank[a][:].rearrange("p (j n) -> p j n", j=2), ACT.Square), "hid_done")
                elif what == "down" and g == GROUPS - 1:
                    wait(act, "down_done", p)
                    signal(nc.scalar.copy(accs[:], acc_bank[:, 0:N]), "acc_copied")
                    wait(act, "out_ready", p)
                    signal(act.dma_start(out[bass.ds(p * T, T)].rearrange("t s c -> s t c"), y_out[:]), "stored")

            run(act, front, expert)
            act.wait_ge(sems["stored"], 16 * STEPS + 16)

        @block.vector
        def _(dve):
            V_ = nc.vector
            chain = [0]

            def mark(instruction):
                chain[0] += 1
                instruction.then_inc(one["dve_chain"], 1)

            def own():
                dve.wait_ge(one["dve_chain"], chain[0])

            def link(instruction):
                mark(instruction)
                own()

            dve.wait_ge(one["ident_ready"], 2)
            link(V_.tensor_copy(ident_r[:], ident[:]))
            dve.wait_ge(one["consts"], 7)
            V_.tensor_copy(ones2[:], ones2f[:]).then_inc(one["identr_ready"], 1)
            dve.wait_ge(one["w_T"], 7)
            for n, (w, r, c) in enumerate(small_T):
                src = F[n % 3][0:c, 128 * (n // 3):128 * (n // 3) + r]
                if w == W_R0 or w == W_R1:
                    hi, lo = (r0_hi, r0_lo) if w == W_R0 else (r1_hi, r1_lo)
                    link(V_.tensor_copy(hi[:], src))
                    mark(V_.tensor_tensor(lo[:], src, hi[:].bitcast(F32), ALU.subtract))
                else:
                    dst = {W_MERGE: merge_T, W_PW: pw_T, W_OUT: outw_T, W_FFD: ffd_T, W_FFU: ffu_T}[w]
                    mark(V_.tensor_copy(dst[:], src))
            own()
            dve.wait_ge(one["gate_ready"], 1)
            for n, (r, g) in enumerate(((0, 0), (3, 2), (4, 1))):
                mark(V_.tensor_scalar(grows[:, n, :], rows[:, r, :], tg[:, g:g + 1], None, ALU.mult))
            mark(V_.tensor_scalar(pwb[:, 1:2], pwb[:, 0:1], 0.5, None, ALU.mult))
            link(V_.tensor_copy(eb_hi[:], eb[:]))
            V_.scalar_tensor_tensor(eb2[:], eb_hi[:].bitcast(F32), neg_row1[:], eb[:],
                                    ALU.mult, ALU.add).then_inc(one["rows_ready"], 1)
            for c in range(2):
                dve.wait_ge(one["e_hi"], c + 1)
                V_.tensor_tensor(exp_lo[:, c * 512:(c + 1) * 512], z_bank[c][:],
                                 exp_hi[:, c * 512:(c + 1) * 512].bitcast(F32), ALU.subtract).then_inc(one["e_lo"], 1)

            def variance(src):
                for t in range(T):
                    mark(V_.bn_stats(bn[:, t, :], src[:, t, :]))
                own()
                for t in range(T):
                    mark(V_.bn_aggr(mv[:, t, :], bn[:, t, :]))
                own()
                signal(V_.tensor_scalar(veps[:], mv[:, :, 1], 1e-5, None, ALU.add), "ln_var")

            def normalise(dst, src, n, p, name):
                wait(dve, "ln_rstd", p, n + 1)
                for t in range(T):
                    last = V_.tensor_scalar(dst[:, t, :], src[:, t, :], mv[:, t, 0:1], rstd[:, t:t + 1],
                                            ALU.subtract, ALU.mult)
                signal(last, name)

            def front(k, p):
                if k == 0:
                    own()
                    dve.sem_clear(one["dve_chain"])
                    chain[0] = 0
                    wait(dve, "in_loaded", p)
                    variance(x_in)
                    normalise(q_tok, x_in, 0, p, "q_ready")
                elif k == 1:
                    wait(dve, "q_T", p)
                    signal(V_.tensor_copy(qT[:], F[0][:, 0:N]), "qT_copied")
                elif k == 2:
                    wait(dve, "scores", p)
                    link(V_.tensor_scalar(att[:], F[2][:, 0:T * LK].rearrange("p (t k) -> p t k", t=T), SCALE, None, ALU.mult))
                    link(V_.copy_predicated(att[:], mask_in[:], neg_inf[:]))
                    link(V_.tensor_reduce(mx[:], att[:], AX_X, ALU.max))
                    signal(V_.tensor_scalar(nmx[:], mx[:], -1.0, None, ALU.mult), "scores_masked")
                    wait(dve, "att_exp", p)
                    link(V_.reciprocal(rs[:], psum_t[:]))
                    signal(V_.tensor_tensor(att[:], att[:], rs[:].unsqueeze(2).broadcast_to([P, T, LK]), ALU.mult), "att_ready")
                elif k == 4:
                    wait(dve, "Y_done", p)
                    wait(dve, "xb_ready", p)
                    signal(V_.scalar_tensor_tensor(x1[:], F[0][:, 0:N].rearrange("p (t c) -> p t c", t=T), tg[:, 0:1], xb[:],
                                                   ALU.mult, ALU.add), "x1_ready")
                    wait(dve, "x1_ready", p)
                elif k == 5:
                    variance(x1)
                    normalise(q_tok, x1, 1, p, "u_ready")
                elif k == 6:
                    wait(dve, "u_T", p)
                    link(V_.tensor_copy(ucv[:, :, KD - 1:], F[2][:, 0:N].rearrange("p (t s) -> p t s", t=T)))
                    link(V_.tensor_scalar(cv[:], ucv[:, :, KD - 1:], dwk[:, KD - 1:KD], dwb[:], ALU.mult, ALU.add))
                    link(V_.scalar_tensor_tensor(cv[:], ucv[:, :, 1:1 + P], dwk[:, 1:2], cv[:], ALU.mult, ALU.add))
                    signal(V_.scalar_tensor_tensor(cv[:], ucv[:, :, 0:P], dwk[:, 0:1], cv[:], ALU.mult, ALU.add), "conv_ready")
                elif k == 7:
                    wait(dve, "pw_tanh", p)
                    link(V_.scalar_tensor_tensor(th[:], th[:], 1.0, zh[:], ALU.add, ALU.mult))
                    link(V_.tensor_tensor(yT[:].rearrange("p (t s) -> p t s", t=T), th[:].rearrange("p (t s) -> p t s", t=T),
                                          ucv[:, :, KD - 1:], ALU.add))
                    link(V_.tensor_copy(y_hi[:], yT[:]))
                    signal(V_.tensor_tensor(y_lo[:], yT[:], y_hi[:].bitcast(F32), ALU.subtract), "y_ready")
                elif k == 8:
                    wait(dve, "logits0", p)
                    link(V_.tensor_tensor(lv[:, :, 0:E0], F[2][:, 0:T * E0].rearrange("p (t e) -> p t e", t=T),
                                          r0b[:].unsqueeze(1).broadcast_to([P, T, E0]), ALU.add))
                    for t in range(T):
                        mark(V_.max(top[:, t, 0:8], lv[:, t, 0:E0]))
                    own()
                    signal(V_.tensor_tensor(rw[:], lv[:, :, 0:E0], top[:, :, 0:1].broadcast_to([P, T, E0]), ALU.subtract), "lmax_ready")
                    for t in range(T):
                        mark(V_.match_replace(mr[:, t, :], top[:, t, :].rearrange("p (a b) -> p a b", b=8)[:, :, 0:2],
                                              lv[:, t, :], PICKED))
                    own()
                    wait(dve, "lexp", p)
                    link(V_.scalar_tensor_tensor(rw[:], mr[:, :, 0:E0], IS_PICKED, rw[:], ALU.is_ge, ALU.mult))
                    link(V_.tensor_reduce(psum_t[:], rw[:], AX_X, ALU.add))
                    link(V_.reciprocal(rs[:], psum_t[:]))
                    signal(V_.scalar_tensor_tensor(rw[:], rw[:], 0.5, rs[:].unsqueeze(2).broadcast_to([P, T, E0]), ALU.mult, ALU.mult), "rw_ready")
                elif k == 9:
                    for c in range(2 * T):
                        wait(dve, "ez_tanh", p, c + 1)
                        if c >= 2:
                            wait(dve, "ew_ready", p, c - 1)
                        signal(V_.scalar_tensor_tensor(eg[:, c % 2, :], eth[:, c % 2, :], 1.0, F[c % 2][:], ALU.add, ALU.mult), "eg_ready")
                    wait(dve, "ew_ready", p)
                    for t in range(T):
                        last = V_.tensor_reduce(acc0[:, t, :], ew[:, t, :].rearrange("p (e o) -> p o e", o=P), AX_X, ALU.add)
                    signal(last, "comb_ready")
                elif k == 10:
                    wait(dve, "hp_done", p)
                    signal(V_.tensor_tensor(hp[:], F[0][:, 0:N].rearrange("p (t c) -> p t c", t=T),
                                            rows[:, 1:2, :].broadcast_to([P, T, P]), ALU.add), "hp_ready")
                elif k == 11:
                    wait(dve, "ssq_ready", p)
                    signal(V_.tensor_scalar(veps[:], ssq[:], 1.0 / D, 1e-6, ALU.mult, ALU.add), "ln_var")
                    wait(dve, "ln_rstd", p, 3)
                    for t in range(T):
                        last = V_.scalar_tensor_tensor(h[:, t, :], hp[:, t, :], rstd[:, t:t + 1], rows[:, 2, :], ALU.mult, ALU.mult)
                    signal(last, "h_ready")
                elif k == 13:
                    wait(dve, "ffu_done", p)
                    link(V_.tensor_tensor(acc0[:], F[0][:, 0:N].rearrange("p (t c) -> p t c", t=T), h[:], ALU.add))
                    wait(dve, "x1b_ready", p)
                    signal(V_.scalar_tensor_tensor(x2[:], acc0[:], tg[:, 2:3], x1b[:], ALU.mult, ALU.add), "x2_ready")
                elif k == 14:
                    wait(dve, "x2_ready", p)
                    variance(x2)
                    normalise(q_tok, x2, 3, p, "q2_ready")
                elif k == 16:
                    wait(dve, "scores2", p)
                    link(V_.tensor_reduce(mx[:], F[0][:, 0:T * LK].rearrange("p (t k) -> p t k", t=T), AX_X, ALU.max))
                    signal(V_.tensor_scalar(nmx[:], mx[:], -SCALE, None, ALU.mult), "max2_ready")
                    wait(dve, "exp2", p)
                    link(V_.reciprocal(rs[:], psum_t[:]))
                    link(V_.tensor_scalar(rs[:], rs[:], tg[:, 1:2], None, ALU.mult))
                elif k == 18:
                    wait(dve, "H_done", p)
                    wait(dve, "x2b_ready", p)
                    for t in range(T):
                        mark(V_.scalar_tensor_tensor(x3[:, t, :], F[2][:, t * P:(t + 1) * P], rs[:, t:t + 1], x2b[:, t, :],
                                                     ALU.mult, ALU.add))
                    own()
                    variance(x3)
                    normalise(xf, x3, 4, p, "xf_ready")
                elif k == 19:
                    wait(dve, "xf_T", p)
                    wait(dve, "z_done", p - 1)
                    link(V_.tensor_copy(x_hi[:], F[1][:, 0:N]))
                    signal(V_.tensor_tensor(x_lo[:], F[1][:, 0:N], x_hi[:].bitcast(F32), ALU.subtract), "x_split")
                elif k == 20:
                    route(p)
                elif k == 21:
                    hand_over(p)

            def route(p):
                wait(dve, "nexp", p)
                link(V_.tensor_scalar(sg[:], sg[:], 1.0, None, ALU.add))
                link(V_.reciprocal(sg[:], sg[:]))
                link(V_.tensor_tensor(sfc[:], sg[:], r1b[:].unsqueeze(1).broadcast_to([P, T, E1]), ALU.add))
                for t in range(T):
                    for g in range(G8):
                        mark(V_.max(g8[:, t, g, :], sfc[:, t, g * EG:(g + 1) * EG]))
                own()
                link(V_.tensor_tensor(gv[:, :, 0:G8], g8[:, :, :, 0], g8[:, :, :, 1], ALU.add))
                for t in range(T):
                    mark(V_.max(gtop[:, t, 0:8], gv[:, t, 0:G8]))
                own()
                for t in range(T):
                    mark(V_.match_replace(gmr[:, t, :], gtop[:, t, :].rearrange("p (a b) -> p a b", b=8)[:, :, 0:TOPG],
                                          gv[:, t, :], PICKED))
                own()
                for t in range(T):
                    mark(V_.scalar_tensor_tensor(
                        masked[:, t, :].rearrange("p (g e) -> p g e", g=G8),
                        gmr[:, t, 0:G8].unsqueeze(2).broadcast_to([P, G8, EG]), IS_PICKED,
                        sfc[:, t, :].rearrange("p (g e) -> p g e", g=G8), ALU.is_ge, ALU.mult))
                own()
                for t in range(T):
                    mark(V_.max(etop[:, t, :], masked[:, t, :]))
                own()
                for t in range(T):
                    mark(V_.match_replace(emr[:, t, :], etop[:, t, :], masked[:, t, :], PICKED))
                own()
                link(V_.scalar_tensor_tensor(cw[:], emr[:], IS_PICKED, sg[:], ALU.is_ge, ALU.mult))
                link(V_.tensor_reduce(cs[:], cw[:], AX_X, ALU.add))
                link(V_.tensor_scalar(cs[:], cs[:], 1e-20, None, ALU.add))
                link(V_.reciprocal(rs[:], cs[:]))
                link(V_.scalar_tensor_tensor(cw[:], cw[:], 2.5, rs[:].unsqueeze(2).broadcast_to([P, T, E1]), ALU.mult, ALU.mult))
                link(V_.tensor_scalar(ry[:].bitcast(I32), cw[:].bitcast(I32), -0.5, RSQRT_MAGIC, ALU.mult, ALU.add))
                for _ in range(3):
                    link(V_.tensor_tensor(ra[:], ry[:], cw[:], ALU.mult))
                    link(V_.scalar_tensor_tensor(rb[:], ra[:], -0.5, ry[:], ALU.mult, ALU.mult))
                    link(V_.scalar_tensor_tensor(ry[:], rb[:], 1.5, ry[:], ALU.add, ALU.mult))

            def hand_over(p):
                wait(dve, "out_ready", p - 1)
                link(V_.tensor_copy(x3m[:], x3[:]))
                signal(V_.tensor_tensor(sc[:], ry[:], cw[:], ALU.mult), "sc_ready")

            def expert(what, g, p):
                if what == "up":
                    if g == 0:
                        wait(dve, "sc_ready", p)
                    for t in range(T):
                        wait(dve, "z_done", p, g * T + t + 1)
                        if g >= 2:
                            wait(dve, "uT_done", p, 2 * (g - 1))
                        w = len(blocks_of(g)) * P
                        if g < ROUTED:
                            signal(V_.scalar_tensor_tensor(
                                u[:, g % 2, t, :].rearrange("p (e i) -> p e i", i=HI),
                                z_bank[t][:].rearrange("p (e i) -> p e i", i=HI), 0.0,
                                sc[:, t, g * EPG:(g + 1) * EPG].unsqueeze(2).broadcast_to([P, EPG, HI]),
                                ALU.max, ALU.mult), "u_done")
                        else:
                            signal(V_.tensor_scalar(u[:, g % 2, t, 0:w], z_bank[t][:, 0:w], 0.0, None, ALU.max), "u_done")
                elif what == "down" and g == GROUPS - 1:
                    wait(dve, "acc_T", p)
                    wait(dve, "stored", p)
                    signal(V_.scalar_tensor_tensor(y_out[:], uT_bank[1][:, 0:N].rearrange("p (t c) -> p t c", t=T), tg[:, 3:4], x3m[:],
                                                   ALU.mult, ALU.add), "out_ready")

            run(dve, front, expert)

        @block.tensor
        def _(pe):
            mm = nc.tensor.matmul

            def transposes(dst, pairs):
                for n, (src, w) in enumerate(pairs):
                    last = nc.tensor.transpose(dst(n), src, ident[0:w, 0:w])
                return last

            def split3(dst, a, b, start=True, stop=True):
                mm(dst, a[0], b[0], start=start, stop=False)
                mm(dst, a[0], b[1], start=False, stop=False)
                return mm(dst, a[1], b[0], start=False, stop=stop)

            pe.wait_ge(one["ident_ready"], 2)
            pe.wait_ge(one["w_loaded"], 16 * 7)
            for n, (w, r, c) in enumerate(small_T):
                nc.tensor.transpose(F[n % 3][0:c, 128 * (n // 3):128 * (n // 3) + r], stage_w[0:r, w, 0:c],
                                    ident[0:r, 0:r]).then_inc(one["w_T"], 1)
            pe.wait_ge(one["e_loaded"], 16)
            for c in range(2):
                for e in range(4):
                    last = nc.tensor.transpose(z_bank[c][:, e * P:(e + 1) * P], stage_e[:, 4 * c + e, :], ident[:])
                last.then_inc(one["e_T"], 1)
            pe.wait_ge(one["rows_ready"], 1)
            pe.wait_ge(one["identr_ready"], 1)
            pe.wait_ge(one["e_lo"], 2)

            def front(k, p):
                if k == 0:
                    wait(pe, "in_loaded", p)
                    wait(pe, "x_split", p - 1)
                    for t in range(T):
                        last = nc.tensor.transpose(F[1][:, t * LK:(t + 1) * LK], ctx_in[:, t, :], ident[0:LK, 0:LK])
                    signal(last, "ctx_T")
                    wait(pe, "q_ready", p)
                    wait(pe, "nexp", p - 1)
                    for t in range(T):
                        last = nc.tensor.transpose(F[0][:, t * P:(t + 1) * P], q_tok[:, t, :], ident[:])
                    signal(last, "q_T")
                elif k == 1:
                    wait(pe, "qT_copied", p)
                    wait(pe, "ctxT_copied", p)
                    for t in range(T):
                        last = mm(F[2][:, t * LK:(t + 1) * LK], qT[:, t * P:(t + 1) * P], ctxT[:, t * LK:(t + 1) * LK],
                                  start=True, stop=True)
                    signal(last, "scores")
                    mm(F[0][:, 0:T * LK], wk[:], ctxT[:], start=True, stop=True)
                    for t in range(T):
                        last = mm(F[1][0:LK, t * P:(t + 1) * P], ctxT[:, t * LK:(t + 1) * LK], wv[:], start=True, stop=True)
                    signal(last, "kv_done")
                elif k == 2:
                    wait(pe, "att_ready", p)
                    for t in range(T):
                        last = mm(F[2][0:LK, t * P:(t + 1) * P], att[:, t, :], merge_T[:], start=True, stop=True)
                    signal(last, "G_done")
                elif k == 3:
                    wait(pe, "G_copied", p)
                    wait(pe, "kv_copied", p)
                    for t in range(T):
                        last = mm(F[0][:, t * P:(t + 1) * P], ctx_in[:, t, :], G[:, t, :], start=True, stop=True)
                    signal(last, "Y_done")
                elif k == 5:
                    wait(pe, "u_ready", p)
                    for t in range(T):
                        last = nc.tensor.transpose(F[2][:, t * P:(t + 1) * P], q_tok[:, t, :], ident[:])
                    signal(last, "u_T")
                elif k == 6:
                    wait(pe, "conv_ready", p)
                    signal(mm(F[1][:, 0:N], pw_T[:], cv[:].rearrange("p t s -> p (t s)"), start=True, stop=True), "pw_done")
                elif k == 7:
                    wait(pe, "y_ready", p)
                    for t in range(T):
                        ts = slice(t * P, (t + 1) * P)
                        last = split3(F[2][:, t * E0:(t + 1) * E0], (y_hi[:, ts], y_lo[:, ts]), (r0_hi[:], r0_lo[:]))
                    signal(last, "logits0")
                elif k == 9:
                    for c in range(2 * T):
                        t, half = divmod(c, 2)
                        ts, cs_ = slice(t * P, (t + 1) * P), slice(half * 512, (half + 1) * 512)
                        if c >= 2:
                            wait(pe, "eg_ready", p, c - 1)
                        mm(F[c % 2][:], ones2[:], eb2[:, cs_], start=True, stop=False)
                        signal(split3(F[c % 2][:], (y_hi[:, ts], y_lo[:, ts]), (exp_hi[:, cs_], exp_lo[:, cs_]), start=False), "ez_done")
                    wait(pe, "comb_ready", p)
                    for t in range(T):
                        last = nc.tensor.transpose(F[2][:, t * P:(t + 1) * P], acc0[:, t, :], ident[:])
                    signal(last, "comb_T")
                elif k == 10:
                    wait(pe, "comb_copied", p)
                    for t in range(T):
                        ts = slice(t * P, (t + 1) * P)
                        mm(F[0][:, ts], combT[:, ts], outw_T[:], start=True, stop=False)
                        mm(F[0][:, ts], y_hi[:, ts], ident_r[:], start=False, stop=False)
                        last = mm(F[0][:, ts], y_lo[:, ts], ident_r[:], start=False, stop=True)
                    signal(last, "hp_done")
                elif k == 11:
                    wait(pe, "h_ready", p)
                    for t in range(T):
                        last = nc.tensor.transpose(F[1][:, t * P:(t + 1) * P], h[:, t, :], ident[:])
                    signal(last, "h_T")
                elif k == 12:
                    wait(pe, "hT_copied", p)
                    signal(mm(F[2][0:HID, 0:N], ffd_T[:], hT[:], start=True, stop=True), "ffd_done")
                elif k == 13:
                    wait(pe, "gelu_ready", p)
                    for t in range(T):
                        last = mm(F[0][:, t * P:(t + 1) * P], gl[:, t * P:(t + 1) * P], ffu_T[:], start=True, stop=True)
                    signal(last, "ffu_done")
                elif k == 14:
                    wait(pe, "q2_ready", p)
                    for t in range(T):
                        last = nc.tensor.transpose(F[1][:, t * P:(t + 1) * P], q_tok[:, t, :], ident[:])
                    signal(last, "q2_T")
                elif k == 15:
                    wait(pe, "q2T_copied", p)
                    signal(mm(F[2][:, 0:N], wq[:], qT[:], start=True, stop=True), "QT_done")
                    wait(pe, "QT_copied", p)
                    for t in range(T):
                        last = mm(F[0][:, t * LK:(t + 1) * LK], QT[:, t * P:(t + 1) * P], KT[:, t * LK:(t + 1) * LK],
                                  start=True, stop=True)
                    signal(last, "scores2")
                elif k == 16:
                    wait(pe, "exp2", p)
                    for t in range(T):
                        last = nc.tensor.transpose(F[1][0:LK, t * P:(t + 1) * P], att[:, t, :], ident[:])
                    signal(last, "P_T")
                elif k == 17:
                    wait(pe, "PT_copied", p)
                    for t in range(T):
                        last = mm(F[2][:, t * P:(t + 1) * P], PT[:, t, :], V[:, t, :], start=True, stop=True)
                    signal(last, "H_done")
                elif k == 18:
                    wait(pe, "xf_ready", p)
                    for t in range(T):
                        last = nc.tensor.transpose(F[1][:, t * P:(t + 1) * P], xf[:, t, :], ident[:])
                    signal(last, "xf_T")
                elif k == 19:
                    wait(pe, "x_split", p)
                    for t in range(T):
                        ts = slice(t * P, (t + 1) * P)
                        last = split3(F[0][:, t * E1:(t + 1) * E1], (x_hi[:, ts], x_lo[:, ts]), (r1_hi[:], r1_lo[:]))
                    signal(last, "logits1")

            def expert(what, g, p):
                nb = len(blocks_of(g))
                if what == "up":
                    w = nb * P
                    for t in range(T):
                        if g:
                            wait(pe, "u_done", p, (g - 1) * T + t + 1)
                        ts, hs = slice(t * P, (t + 1) * P), slice(g * GW, g * GW + w)
                        if g == 0 and t == 0:
                            pe.wait_ge(one["up_l"], len(UP_SPLIT_AT))
                        signal(split3(z_bank[t][:, 0:w], (x_hi[:, ts], x_lo[:, ts]), (up_hi[:, hs], up_lo[:, hs])), "z_done")
                elif what == "tr":
                    for a in range((nb + 1) // 2):
                        wait(pe, "u_done", p, (g + 1) * T)
                        if g:
                            wait(pe, "hid_done", p, 2 * (g - 1) + a + 1)
                        for j in range(2):
                            for t in range(T):
                                b = 2 * a + j
                                last = nc.tensor.transpose(uT_bank[a][:, j * N + t * P:j * N + (t + 1) * P],
                                                           u[:, g % 2, t, b * P:(b + 1) * P], ident[:])
                        signal(last, "uT_done")
                elif what == "down":
                    wait(pe, "hid_done", p, min(2 * g + 2, per["hid_done"]))
                    if g == 0:
                        pe.wait_ge(one["d_loaded"], 48)
                    for j, b in enumerate(blocks_of(g)):
                        last = mm(acc_bank[:, 0:N], down_sb[:, b, :], hid[:, g % 2, j, :],
                                  start=(b == 0), stop=(b == NBLK - 1))
                    signal(last, "down_done")
                    if g == GROUPS - 1:
                        wait(pe, "acc_copied", p)
                        for t in range(T):
                            last = nc.tensor.transpose(uT_bank[1][:, t * P:(t + 1) * P], accs[:, t * P:(t + 1) * P], ident[:])
                        signal(last, "acc_T")

            run(pe, front, expert)


_INS = [
    "x", "ctx_1024", "mask_BxSxS2_bk1", "g_xattn", "g_ffn", "L0_xattn_W_merge", "L0_xattn_b_merge",
    "L0_ffn_dw_kernel", "L0_ffn_dw_bias", "L0_ffn_pw_w", "L0_ffn_pw_b", "L0_ffn_router_w", "L0_ffn_router_b",
    "L0_ffn_expert_w", "L0_ffn_expert_b", "L0_ffn_out_w", "L0_ffn_out_b", "L0_ffn_norm_w", "L0_ffn_ff_down_w",
    "L0_ffn_ff_down_b", "L0_ffn_ff_up_w", "L0_ffn_ff_up_b", "L1_xattn_W_q", "L1_xattn_b_q", "L1_xattn_W_k",
    "L1_xattn_b_k", "L1_xattn_W_v", "L1_xattn_b_v", "L1_ffn_router_w", "L1_ffn_correction_bias", "L1_ffn_up_w",
    "L1_ffn_down_w", "L1_ffn_shared_up_w", "L1_ffn_shared_down_w",
]


def kernel(**inputs):
    import numpy as _np
    import concourse.bacc as _bacc
    from concourse import mybir as _mybir
    from concourse.bass_utils import run_bass_kernel_spmd as _run

    nc = _bacc.Bacc("TRN2", target_bir_lowering=False, num_devices=1)
    arrays, args = {}, []
    for name in _INS:
        a = _np.ascontiguousarray(inputs[name])
        arrays[f"in_{name}"] = a
        args.append(nc.dram_tensor(f"in_{name}", a.shape, _mybir.dt.from_np(a.dtype), kind="ExternalInput").ap())
    out = nc.dram_tensor("out_x", inputs["x"].shape, _mybir.dt.float32, kind="ExternalOutput").ap()
    flamingo_kernel(nc, *args, out)
    r = _run(nc, [arrays], core_ids=[0])
    return r.results[0]["out_x"]
```
